# Optimizing a Trainium2 kernel written in Bass

```python
import numpy as np
import jax
import jax.numpy as jnp

def _softmax(x, axis=-1):
    return jax.nn.softmax(x, axis=axis)

def _gelu(x):
    return jax.nn.gelu(x, approximate=True)

def _silu(x):
    return jax.nn.silu(x)

def _sigmoid(x):
    return jax.nn.sigmoid(x)

def _layernorm(x, axis=-1, eps=1e-05):
    m = jnp.mean(x, axis=axis, keepdims=True)
    v = jnp.var(x, axis=axis, keepdims=True)
    return (x - m) / jnp.sqrt(v + eps)

def _scatter_add(tgt, idx, src, axis=0):
    return tgt.at[idx].add(src)

def _segment_sum(src, seg, n):
    return jax.ops.segment_sum(src, seg, n)
kernel_name = 'mk_adj_resnorm_d1_adj_r2_c5ffcf'

def setup_inputs(seed: int=0):
    np.random.seed(seed)
    _w = jnp.asarray

    def _rec_inputs():
        import jax
        import jax.numpy as jnp
        _gk = jax.random.key(seed)
        x = -0.000929 + 1 * jax.random.normal(jax.random.fold_in(_gk, 1), (8192, 64), jnp.float32)
        _w = (1.0 + jnp.arange(8192, dtype=jnp.float32)) ** (-0.5)
        _w = _w / _w.mean()
        _pij = jnp.clip(0.00195312 * _w[:, None] * _w[None, :], 0.0, 1.0)
        _a = jax.random.uniform(jax.random.fold_in(_gk, 2), (8192, 8192)) < _pij
        _a = jnp.logical_or(_a, jnp.eye(8192, dtype=bool))
        _af = _a.astype(jnp.float32)
        _af = _af * jax.random.uniform(jax.random.fold_in(_gk, 3), (8192, 8192), jnp.float32, 0.05, 1)
        adj = _af
        return (x, adj)
    x, adj = _rec_inputs()

    def _L0_gnn_setup():
        import jax, jax.numpy as jnp
        import numpy as np
        P_DROP = 0.1
        key = jax.random.key(seed)
        k1, k2, k3 = jax.random.split(key, 3)
        N, D = (8192, 64)
        x = jax.random.normal(k1, (N, D), dtype=jnp.float32)
        adj = jax.random.uniform(k2, (N, N), dtype=jnp.float32)
        u = jax.random.uniform(k3, (N, D), dtype=jnp.float32)
        return {'x': x, 'adj': adj, 'u': u}
    _L0_gnn_all = _L0_gnn_setup()
    _L0_gnn_in = {k: v for k, v in _L0_gnn_all.items() if k in ('u',)}
    del _L0_gnn_all
    return {'x': x, 'adj': adj, 'L0_gnn_u': _L0_gnn_in['u']}

def reference(x, adj, L0_gnn_u):
    import jax
    import jax.numpy as jnp

    def _L0_gnn_ref(x, adj, u):
        import jax, jax.numpy as jnp
        import numpy as np
        P_DROP = 0.1
        keep = (u >= P_DROP).astype(x.dtype)
        x_drop = x * keep / (1.0 - P_DROP)
        return jnp.matmul(adj, x_drop)
    x = _layernorm(x + _L0_gnn_ref(x, adj, L0_gnn_u), axis=-1)
    return x

_drawn_inputs = setup_inputs


def setup_inputs(seed=0):
    import zlib

    import numpy as np

    out = dict(_drawn_inputs(seed))
    spreads = {}
    factors = {}
    for name, (base, spread) in spreads.items():
        noise = np.random.default_rng([zlib.crc32(name.encode()), seed]).standard_normal(out[name].shape)
        drawn = base * np.exp(spread * noise) if base else spread * noise
        out[name] = jnp.asarray(drawn.astype(out[name].dtype))
    for name, factor in factors.items():
        out[name] = (out[name] * factor).astype(out[name].dtype)
    return out
```

```python
from contextlib import ExitStack

import concourse.bass as bass
from concourse import mybir

P = 128
N = 8192
D = 64
ROWS = N // P
HALF = 512
CHUNK = 2 * HALF
CHUNKS = N // CHUNK
CB = CHUNK // P
TB = 4
TILES = ROWS // TB
SLOTS = 8
ROUNDS = CHUNKS * TILES // SLOTS
XPARTS = 4
XB = ROWS // XPARTS
P_DROP = 0.1
EPS = 1e-5


def build(nc, x, adj_tiles, u, out):
    f32 = mybir.dt.float32
    ALU = mybir.AluOpType
    ACT = mybir.ActivationFunctionType
    AX = mybir.AxisListType

    x_rows = x.rearrange("(p b) d -> p (b d)", p=P)
    u_rows = u.rearrange("(p b) d -> p (b d)", p=P)
    out_rows = out.rearrange("(p b) d -> p (b d)", p=P)

    with ExitStack() as ctx:
        def sb(name, shape):
            return ctx.enter_context(nc.sbuf_tensor(name, shape, f32))

        def sem(name):
            return ctx.enter_context(nc.semaphore(name))

        adj_ring = sb("adj_ring", [P, SLOTS, TB, CHUNK])
        x_sb = sb("x_sb", [P, ROWS * D])
        xd = sb("xd", [P, ROWS, D])
        xd_flat = xd[:, :, :].rearrange("p b d -> p (b d)")
        ident = sb("ident", [P, P])
        aggT = sb("aggT", [P, 2, HALF])
        z = sb("z", [P, 2, CB, D])
        y = sb("y", [P, 2, CB, D])
        sq = sb("sq", [P, CB, D])
        row_sum = sb("row_sum", [P, CB])
        sq_sum = sb("sq_sum", [P, CB])
        var = sb("var", [P, CB])
        std = sb("std", [P, CB])
        rstd = sb("rstd", [P, CB])
        acc = [ctx.enter_context(nc.psum_tensor(f"acc{i}", [P, HALF], f32)) for i in range(2)]
        agg = [ctx.enter_context(nc.psum_tensor(f"agg{i}", [P, CB * D], f32)) for i in range(2)]

        x_loaded = [sem(f"x_loaded{i}") for i in range(XPARTS)]
        adj_loaded = [sem(f"adj_loaded{i}") for i in range(SLOTS)]
        tile_used = sem("tile_used")
        mask_ready = sem("mask_ready")
        xd_ready = sem("xd_ready")
        ident_zero = sem("ident_zero")
        ident_ready = sem("ident_ready")
        acc_copied = sem("acc_copied")
        agg_ready = sem("agg_ready")
        dve_step = sem("dve_step")
        squares_ready = sem("squares_ready")
        std_ready = sem("std_ready")
        out_stored = sem("out_stored")

        RESID, SUM, CENTER, SQSUM, VAR, RSTD, SCALE = range(1, 8)
        DVE_STEPS = 7

        block = ctx.enter_context(nc.Block())

        @block.sync
        def _(sp):
            for i in range(XPARTS):
                part = slice(i * XB * D, (i + 1) * XB * D)
                sp.dma_start(xd_flat[:, part], u_rows[:, part]).then_inc(x_loaded[i], 16)
                sp.dma_start(x_sb[:, part], x_rows[:, part]).then_inc(x_loaded[i], 16)
                if i == 0:
                    sp.dma_start(adj_ring[:, 0], adj_tiles[0]).then_inc(adj_loaded[0], 16)
            for s in range(1, SLOTS):
                sp.dma_start(adj_ring[:, s], adj_tiles[s]).then_inc(adj_loaded[s], 16)
            with sp.Fori(1, ROUNDS) as r:
                for s in range(SLOTS):
                    sp.wait_ge(tile_used, (r - 1) * SLOTS + s + 1)
                    sp.dma_start(adj_ring[:, s], adj_tiles[r * SLOTS + s]).then_inc(adj_loaded[s], 16)

        @block.gpsimd
        def _(pool):
            nc.gpsimd.memset(ident[:, :], 0.0).then_inc(ident_zero, 1)
            pool.wait_ge(ident_zero, 1)
            nc.gpsimd.affine_select(out=ident[:, :], in_=ident[:, :], compare_op=ALU.not_equal, fill=1.0,
                                    base=0, pattern=[[-1, P]], channel_multiplier=1).then_inc(ident_ready, 1)

        def multiply(pe, g, bank):
            for t in range(TILES):
                pe.wait_ge(adj_loaded[t % SLOTS], (g * (TILES // SLOTS) + t // SLOTS + 1) * 16)
                for b in range(TB):
                    k = t * TB + b
                    for h in range(2):
                        last = nc.tensor.matmul(bank[h * D:(h + 1) * D, :], xd[:, k, :],
                                                adj_ring[:, t % SLOTS, b, h * HALF:(h + 1) * HALF],
                                                start=(k == 0), stop=(k == ROWS - 1))
                last.then_inc(tile_used, 1)

        def turn_back(pe, g, par):
            pe.wait_ge(acc_copied, g + 1)
            for k in range(HALF // P):
                last = nc.tensor.transpose(agg[par][:, k * P:(k + 1) * P],
                                           aggT[:, par, k * P:(k + 1) * P], ident[:, :])
            last.then_inc(agg_ready, 1)

        @block.tensor
        def _(pe):
            pe.wait_ge(ident_ready, 1)
            pe.wait_ge(xd_ready, XPARTS)
            with pe.Fori(0, CHUNKS // 2) as gg:
                for par in range(2):
                    multiply(pe, gg * 2 + par, acc[par])
                    turn_back(pe, gg * 2 + par, par)

        @block.scalar
        def _(act):
            with act.Fori(0, CHUNKS // 2) as gg:
                for par in range(2):
                    g = gg * 2 + par
                    act.wait_ge(tile_used, (g + 1) * TILES)
                    nc.scalar.copy(aggT[:, par, :], acc[par][:, :]).then_inc(acc_copied, 1)
                    act.wait_ge(dve_step, g * DVE_STEPS + CENTER)
                    nc.scalar.activation(sq[:, :, :], z[:, par], ACT.Square).then_inc(squares_ready, 1)
                    act.wait_ge(dve_step, g * DVE_STEPS + VAR)
                    nc.scalar.activation(std[:, :], var[:, :], ACT.Sqrt).then_inc(std_ready, 1)
                    act.wait_ge(dve_step, g * DVE_STEPS + SCALE)
                    rows = bass.ds(g * (CB * D), CB * D)
                    act.dma_start(out_rows[:, rows], y[:, par].rearrange("p b d -> p (b d)")).then_inc(out_stored, 16)
                    act.wait_ge(out_stored, (g + 1) * 16)

        @block.vector
        def _(dve):
            for i in range(XPARTS):
                part = slice(i * XB * D, (i + 1) * XB * D)
                dve.wait_ge(x_loaded[i], 32)
                nc.vector.tensor_scalar(xd_flat[:, part], xd_flat[:, part], P_DROP, 1.0 / (1.0 - P_DROP),
                                        ALU.is_ge, ALU.mult).then_inc(mask_ready, 1)
                dve.wait_ge(mask_ready, i + 1)
                nc.vector.tensor_tensor(xd_flat[:, part], x_sb[:, part], xd_flat[:, part],
                                        ALU.mult).then_inc(xd_ready, 1)
            with dve.Fori(0, CHUNKS // 2) as gg:
                for par in range(2):
                    g = gg * 2 + par
                    done = g * DVE_STEPS
                    z3 = z[:, par]

                    def over_d(stat):
                        return stat[:, :].unsqueeze(2).to_broadcast([P, CB, D])

                    dve.wait_ge(agg_ready, g + 1)
                    nc.vector.tensor_tensor(z3, agg[par][:, :].rearrange("p (b d) -> p b d", d=D),
                                            x_sb[:, bass.ds(g * (CB * D), CB * D)].rearrange("p (b d) -> p b d", d=D),
                                            ALU.add).then_inc(dve_step, 1)
                    dve.wait_ge(dve_step, done + RESID)
                    nc.vector.tensor_reduce(row_sum[:, :], z3, AX.X, ALU.add).then_inc(dve_step, 1)
                    dve.wait_ge(dve_step, done + SUM)
                    nc.vector.scalar_tensor_tensor(z3, over_d(row_sum), -1.0 / D, z3,
                                                   ALU.mult, ALU.add).then_inc(dve_step, 1)
                    dve.wait_ge(squares_ready, g + 1)
                    nc.vector.tensor_reduce(sq_sum[:, :], sq[:, :, :], AX.X, ALU.add).then_inc(dve_step, 1)
                    dve.wait_ge(dve_step, done + SQSUM)
                    nc.vector.tensor_scalar(var[:, :], sq_sum[:, :], 1.0 / D, EPS,
                                            ALU.mult, ALU.add).then_inc(dve_step, 1)
                    dve.wait_ge(std_ready, g + 1)
                    nc.vector.reciprocal(rstd[:, :], std[:, :]).then_inc(dve_step, 1)
                    dve.wait_ge(dve_step, done + RSTD)
                    nc.vector.tensor_tensor(y[:, par], z3, over_d(rstd), ALU.mult).then_inc(dve_step, 1)


def kernel(x, adj, L0_gnn_u):
    import numpy as np
    import concourse.bacc as bacc
    from concourse.bass_utils import run_bass_kernel_spmd

    f32 = mybir.dt.float32
    adj_tiles = np.asarray(adj).reshape(P, CHUNKS, HALF // P, 2, P, TILES, TB).transpose(1, 5, 4, 6, 3, 2, 0)
    adj_tiles = np.ascontiguousarray(adj_tiles).reshape(CHUNKS * TILES, P, TB, CHUNK)

    nc = bacc.Bacc("TRN2", target_bir_lowering=False, num_devices=1)
    arrays = {"x": np.ascontiguousarray(x), "adj_tiles": adj_tiles, "u": np.ascontiguousarray(L0_gnn_u)}
    args = [nc.dram_tensor(n, a.shape, f32, kind="ExternalInput").ap() for n, a in arrays.items()]
    out = nc.dram_tensor("out", (N, D), f32, kind="ExternalOutput").ap()
    build(nc, *args, out)
    r = run_bass_kernel_spmd(nc, [arrays], core_ids=[0])
    return r.results[0]["out"]
```

```python
from contextlib import ExitStack

import concourse.bass as bass
from concourse import mybir

P = 128
N = 8192
D = 64
ROWS = N // P
HALF = 512
CHUNK = 2 * HALF
CHUNKS = N // CHUNK
CB = CHUNK // P
TB = 4
TILES = ROWS // TB
SLOTS = 8
LOOPED = CHUNKS - 1
ROUNDS = LOOPED * TILES // SLOTS
NARROW = P
WIDE = HALF - NARROW
NARROW_LOADS = [8, 8, 8, 8, 8, 8, 4, 4, 4, 2, 2]
XPARTS = 4
XB = ROWS // XPARTS
P_DROP = 0.1
EPS = 1e-5


def build(nc, x, adj_tiles, adj_wide, adj_narrow, u, out):
    f32 = mybir.dt.float32
    ALU = mybir.AluOpType
    ACT = mybir.ActivationFunctionType
    AX = mybir.AxisListType

    x_rows = x.rearrange("(p b) d -> p (b d)", p=P)
    u_rows = u.rearrange("(p b) d -> p (b d)", p=P)
    out_rows = out.rearrange("(p b) d -> p (b d)", p=P)

    with ExitStack() as ctx:
        def sb(name, shape):
            return ctx.enter_context(nc.sbuf_tensor(name, shape, f32))

        def sem(name):
            return ctx.enter_context(nc.semaphore(name))

        adj_ring = sb("adj_ring", [P, SLOTS, TB * CHUNK])
        xc = sb("xc", [P, ROWS, D])
        xd = sb("xd", [P, ROWS, D])
        xc_flat = xc[:, :, :].rearrange("p b d -> p (b d)")
        xd_flat = xd[:, :, :].rearrange("p b d -> p (b d)")
        ident = sb("ident", [P, P])
        centre = sb("centre", [P, P])
        eps = sb("eps", [P, 1])
        x_sum = sb("x_sum", [P, ROWS])
        aggT = sb("aggT", [P, HALF])
        sq = sb("sq", [P, CB, D])
        sq_sum = sb("sq_sum", [P, CB])
        std = sb("std", [P, CB])
        rstd = sb("rstd", [P, CB])
        y = sb("y", [P, CB, D])
        acc = ctx.enter_context(nc.psum_tensor("acc", [P, HALF], f32))
        z = ctx.enter_context(nc.psum_tensor("z", [P, CB, D], f32))
        z_flat = z[:, :, :].rearrange("p b d -> p (b d)")

        x_loaded = [sem(f"x_loaded{i}") for i in range(XPARTS)]
        adj_loaded = [sem(f"adj_loaded{i}") for i in range(SLOTS)]
        tile_used = sem("tile_used")
        mask_ready = sem("mask_ready")
        xd_ready = sem("xd_ready")
        x_summed = sem("x_summed")
        ident_zero = sem("ident_zero")
        blocks_set = sem("blocks_set")
        eps_ready = sem("eps_ready")
        ident_ready = sem("ident_ready")
        centre_ready = sem("centre_ready")
        acc_copied = sem("acc_copied")
        z_ready = sem("z_ready")
        squares_ready = sem("squares_ready")
        sq_summed = sem("sq_summed")
        std_ready = sem("std_ready")
        rstd_ready = sem("rstd_ready")
        z_begin = sem("z_begin")
        out_stored = sem("out_stored")

        block = ctx.enter_context(nc.Block())

        @block.sync
        def _(sp):
            for i in range(XPARTS):
                part = slice(i * XB * D, (i + 1) * XB * D)
                sp.dma_start(xd_flat[:, part], u_rows[:, part]).then_inc(x_loaded[i], 16)
                sp.dma_start(xc_flat[:, part], x_rows[:, part]).then_inc(x_loaded[i], 16)
            for s in range(SLOTS):
                sp.dma_start(adj_ring[:, s], adj_tiles[s]).then_inc(adj_loaded[s], 16)
            with sp.Fori(1, ROUNDS) as r:
                for s in range(SLOTS):
                    sp.wait_ge(tile_used, (r - 1) * SLOTS + s + 1)
                    sp.dma_start(adj_ring[:, s], adj_tiles[r * SLOTS + s]).then_inc(adj_loaded[s], 16)
            n = LOOPED * TILES
            for t in range(TILES):
                sp.wait_ge(tile_used, n - SLOTS + 1)
                sp.dma_start(adj_ring[:, n % SLOTS, 0:TB * 2 * WIDE], adj_wide[t]).then_inc(adj_loaded[n % SLOTS], 16)
                n += 1
            first = 0
            for blocks in NARROW_LOADS:
                sp.wait_ge(tile_used, n - SLOTS + 1)
                size = blocks * 2 * NARROW
                sp.dma_start(adj_ring[:, n % SLOTS, 0:size],
                             adj_narrow[first * P:first * P + P * size].rearrange("(p c) -> p c", p=P)
                             ).then_inc(adj_loaded[n % SLOTS], 16)
                first += size
                n += 1

        @block.gpsimd
        def _(pool):
            nc.gpsimd.memset(ident[:, :], 0.0).then_inc(ident_zero, 1)
            pool.wait_ge(ident_zero, 1)
            nc.gpsimd.affine_select(out=ident[:, :], in_=ident[:, :], compare_op=ALU.not_equal, fill=1.0,
                                    base=0, pattern=[[-1, P]], channel_multiplier=1).then_inc(ident_ready, 1)

        def multiply(pe, slot, blocks, first, width):
            for b in range(blocks):
                for h in range(2):
                    col = (b * 2 + h) * width
                    last = nc.tensor.matmul(acc[h * D:(h + 1) * D, 0:width], xd[:, first + b, :],
                                            adj_ring[:, slot, col:col + width],
                                            start=(first + b == 0), stop=(first + b == ROWS - 1))
            last.then_inc(tile_used, 1)

        def start_z(pe, section, row0, width):
            pe.wait_ge(z_begin, section + 1)
            nc.tensor.matmul(z_flat[:, 0:2 * width // P * D], ident[:, :],
                             xc_flat[:, bass.ds(row0 * D, 2 * width // P * D)], start=True, stop=False)

        def turn_back(pe, section, width):
            pe.wait_ge(acc_copied, section + 1)
            for k in range(width // P):
                last = nc.tensor.matmul(z_flat[:, k * P:(k + 1) * P], aggT[:, k * P:(k + 1) * P], centre[:, :],
                                        start=False, stop=(k == width // P - 1))
            last.then_inc(z_ready, 1)

        @block.tensor
        def _(pe):
            pe.wait_ge(ident_ready, 1)
            pe.wait_ge(centre_ready, 1)
            pe.wait_ge(xd_ready, XPARTS)
            with pe.Fori(0, LOOPED) as g:
                for t in range(TILES):
                    pe.wait_ge(adj_loaded[t % SLOTS], (g * (TILES // SLOTS) + t // SLOTS + 1) * 16)
                    if t == TILES - 1:
                        start_z(pe, g, g * CB, HALF)
                    multiply(pe, t % SLOTS, TB, t * TB, HALF)
                turn_back(pe, g, HALF)
            n = LOOPED * TILES
            for t in range(TILES):
                pe.wait_ge(adj_loaded[n % SLOTS], (n // SLOTS + 1) * 16)
                if t == TILES - 1:
                    start_z(pe, LOOPED, LOOPED * CB, WIDE)
                multiply(pe, n % SLOTS, TB, t * TB, WIDE)
                n += 1
            turn_back(pe, LOOPED, WIDE)
            first = 0
            for blocks in NARROW_LOADS:
                if first + blocks == ROWS:
                    start_z(pe, LOOPED + 1, ROWS - 2 * NARROW // P, NARROW)
                pe.wait_ge(adj_loaded[n % SLOTS], (n // SLOTS + 1) * 16)
                multiply(pe, n % SLOTS, blocks, first, NARROW)
                first += blocks
                n += 1
            turn_back(pe, LOOPED + 1, NARROW)

        def act_section(act, section, loads, row0, width):
            cb = 2 * width // P
            act.wait_ge(tile_used, loads)
            nc.scalar.copy(aggT[:, 0:width], acc[:, 0:width]).then_inc(acc_copied, 1)
            act.wait_ge(z_ready, section + 1)
            nc.scalar.activation(sq[:, 0:cb], z[:, 0:cb], ACT.Square).then_inc(squares_ready, 1)
            act.wait_ge(sq_summed, section + 1)
            nc.scalar.activation(std[:, 0:cb], sq_sum[:, 0:cb], ACT.Sqrt,
                                 scale=1.0 / D, bias=eps[:, :]).then_inc(std_ready, 1)
            act.wait_ge(z_begin, section + 2)
            act.dma_start(out_rows[:, bass.ds(row0 * D, cb * D)],
                          y[:, 0:cb].rearrange("p b d -> p (b d)")).then_inc(out_stored, 16)
            act.wait_ge(out_stored, (section + 1) * 16)

        @block.scalar
        def _(act):
            act.wait_ge(eps_ready, 1)
            with act.Fori(0, LOOPED) as g:
                act_section(act, g, (g + 1) * TILES, g * CB, HALF)
            act_section(act, LOOPED, CHUNKS * TILES, LOOPED * CB, WIDE)
            act_section(act, LOOPED + 1, CHUNKS * TILES + len(NARROW_LOADS), ROWS - 2 * NARROW // P, NARROW)

        def dve_section(dve, section, width):
            cb = 2 * width // P
            dve.wait_ge(squares_ready, section + 1)
            nc.vector.tensor_reduce(sq_sum[:, 0:cb], sq[:, 0:cb], AX.X, ALU.add).then_inc(sq_summed, 1)
            dve.wait_ge(std_ready, section + 1)
            nc.vector.reciprocal(rstd[:, 0:cb], std[:, 0:cb]).then_inc(rstd_ready, 1)
            dve.wait_ge(rstd_ready, section + 1)
            nc.vector.tensor_tensor(y[:, 0:cb], z[:, 0:cb], rstd[:, 0:cb].unsqueeze(2).to_broadcast([P, cb, D]),
                                    ALU.mult).then_inc(z_begin, 1)

        @block.vector
        def _(dve):
            nc.vector.memset(eps[:, :], EPS).then_inc(eps_ready, 1)
            for a in range(2):
                for b in range(2):
                    nc.vector.memset(centre[a * D:(a + 1) * D, b * D:(b + 1) * D],
                                     -1.0 / D if a == b else 0.0).then_inc(blocks_set, 1)
            dve.wait_ge(blocks_set, 4)
            dve.wait_ge(ident_ready, 1)
            nc.vector.tensor_tensor(centre[:, :], centre[:, :], ident[:, :], ALU.add).then_inc(centre_ready, 1)
            for i in range(XPARTS):
                part = slice(i * XB * D, (i + 1) * XB * D)
                dve.wait_ge(x_loaded[i], 32)
                nc.vector.tensor_scalar(xd_flat[:, part], xd_flat[:, part], P_DROP, 1.0 / (1.0 - P_DROP),
                                        ALU.is_ge, ALU.mult).then_inc(mask_ready, 1)
                dve.wait_ge(mask_ready, i + 1)
                nc.vector.tensor_tensor(xd_flat[:, part], xc_flat[:, part], xd_flat[:, part],
                                        ALU.mult).then_inc(xd_ready, 1)
            nc.vector.tensor_reduce(x_sum[:, :], xc[:, :, :], AX.X, ALU.add).then_inc(x_summed, 1)
            dve.wait_ge(x_summed, 1)
            dve.wait_ge(xd_ready, XPARTS)
            nc.vector.scalar_tensor_tensor(xc[:, :, :], x_sum[:, :].unsqueeze(2).to_broadcast([P, ROWS, D]),
                                           -1.0 / D, xc[:, :, :], ALU.mult, ALU.add).then_inc(z_begin, 1)
            with dve.Fori(0, LOOPED) as g:
                dve_section(dve, g, HALF)
            dve_section(dve, LOOPED, WIDE)
            dve_section(dve, LOOPED + 1, NARROW)


def kernel(x, adj, L0_gnn_u):
    import numpy as np
    import concourse.bacc as bacc
    from concourse.bass_utils import run_bass_kernel_spmd

    by_block = np.asarray(adj).reshape(P, CHUNKS, HALF // P, 2, P, ROWS).transpose(1, 5, 4, 3, 2, 0)
    looped, last = by_block[:LOOPED], by_block[LOOPED]
    wide = WIDE // P

    def loads(a, blocks):
        a = a.reshape(a.shape[:-5] + (a.shape[-5] // blocks, blocks) + a.shape[-4:])
        return np.ascontiguousarray(np.swapaxes(a, -5, -4))

    adj_tiles = loads(looped, TB).reshape(LOOPED * TILES, P, TB * CHUNK)
    adj_wide = loads(last[:, :, :, :wide], TB).reshape(TILES, P, TB * 2 * WIDE)
    pieces, first = [], 0
    for blocks in NARROW_LOADS:
        pieces.append(loads(last[first:first + blocks, :, :, wide:], blocks).reshape(-1))
        first += blocks
    adj_narrow = np.concatenate(pieces)

    nc = bacc.Bacc("TRN2", target_bir_lowering=False, num_devices=1)
    arrays = {"x": np.ascontiguousarray(x), "adj_tiles": adj_tiles, "adj_wide": adj_wide,
              "adj_narrow": adj_narrow, "u": np.ascontiguousarray(L0_gnn_u)}
    f32 = mybir.dt.float32
    args = [nc.dram_tensor(n, a.shape, f32, kind="ExternalInput").ap() for n, a in arrays.items()]
    out = nc.dram_tensor("out", (N, D), f32, kind="ExternalOutput").ap()
    build(nc, *args, out)
    r = run_bass_kernel_spmd(nc, [arrays], core_ids=[0])
    return r.results[0]["out"]
```
